# Optimizing a Trainium2 kernel written in Bass

```python
import numpy as np
import jax
import jax.numpy as jnp

def _softmax(x, axis=-1):
    return jax.nn.softmax(x, axis=axis)

def _gelu(x):
    return jax.nn.gelu(x, approximate=True)

def _silu(x):
    return jax.nn.silu(x)

def _sigmoid(x):
    return jax.nn.sigmoid(x)

def _layernorm(x, axis=-1, eps=1e-05):
    m = jnp.mean(x, axis=axis, keepdims=True)
    v = jnp.var(x, axis=axis, keepdims=True)
    return (x - m) / jnp.sqrt(v + eps)

def _scatter_add(tgt, idx, src, axis=0):
    return tgt.at[idx].add(src)

def _segment_sum(src, seg, n):
    return jax.ops.segment_sum(src, seg, n)
kernel_name = 'mk_cond_resid_d2_seqx_r2_b44e0b'

def setup_inputs(seed: int=0):
    np.random.seed(seed)
    _w = jnp.asarray

    def _rec_inputs():
        import jax
        import jax.numpy as jnp
        _rk = jax.random.key(seed)
        x = -0.000125 + 0.9999 * jax.random.normal(jax.random.fold_in(_rk, 1), (8, 512, 2048), jnp.float32)
        _lenS = 512 - jax.random.randint(jax.random.fold_in(_rk, 7), (8,), 0, max(1, 512 // 4) + 1, jnp.int32)
        _lenS2 = 512 - jax.random.randint(jax.random.fold_in(_rk, 8), (8,), 0, max(1, 512 // 4) + 1, jnp.int32)
        itok_B_3_7 = jax.random.randint(jax.random.fold_in(_rk, 11), (8,), 3, 8, jnp.int32)
        itok_B_0_15 = jax.random.randint(jax.random.fold_in(_rk, 12), (8,), 0, 16, jnp.int32)
        return (x, itok_B_3_7, itok_B_0_15)
    x, itok_B_3_7, itok_B_0_15 = _rec_inputs()

    def _L0_cond_setup():
        import jax, jax.numpy as jnp
        import numpy as np
        RANK = 16
        ALPHA = 16.0
        SCALING = ALPHA / RANK
        N_ADAPTERS = 8
        IN_F = 2048
        OUT_F = 2048
        BATCH = 4
        SEQ = 1024
        key = jax.random.key(seed)
        kx, ka, kb, ki = jax.random.split(key, 4)
        x = jax.random.normal(kx, (BATCH, SEQ, IN_F), dtype=jnp.float32)
        A = jax.random.normal(ka, (N_ADAPTERS, OUT_F, RANK), dtype=jnp.float32) * 0.02
        B = jax.random.normal(kb, (N_ADAPTERS, RANK, IN_F), dtype=jnp.float32) * 0.02
        adapter_ids = jax.random.randint(ki, (BATCH,), 0, N_ADAPTERS, dtype=jnp.int32)
        return {'x': x, 'A': A, 'B': B, 'adapter_ids': adapter_ids}
    _L0_cond_all = _L0_cond_setup()
    _L0_cond_in = {k: v for k, v in _L0_cond_all.items() if k in ('A', 'B')}
    del _L0_cond_all

    def _L1_cond_setup():
        import jax, jax.numpy as jnp
        import numpy as np
        SCALING = 16.0 / 16
        key = jax.random.key(seed)
        k1, k2, k3, k4, k5 = jax.random.split(key, 5)
        B, S, D_IN, D_OUT, R, N_ADPT = (8, 1024, 2048, 2048, 16, 16)
        x = jax.random.normal(k1, (B, S, D_IN), dtype=jnp.float32)
        adapter_indices = jax.random.randint(k2, (B,), 0, N_ADPT, dtype=jnp.int32)
        W = jax.random.normal(k3, (D_IN, D_OUT), dtype=jnp.float32) * 0.02
        lora_A = jax.random.normal(k4, (N_ADPT, D_IN, R), dtype=jnp.float32) * 0.02
        lora_B = jax.random.normal(k5, (N_ADPT, R, D_OUT), dtype=jnp.float32) * 0.02
        return {'x': x, 'adapter_indices': adapter_indices, 'W': W, 'lora_A': lora_A, 'lora_B': lora_B}
    _L1_cond_all = _L1_cond_setup()
    _L1_cond_in = {k: v for k, v in _L1_cond_all.items() if k in ('W', 'lora_A', 'lora_B')}
    del _L1_cond_all
    return {'x': x, 'itok_B_3_7': itok_B_3_7, 'itok_B_0_15': itok_B_0_15, 'L0_cond_A': _L0_cond_in['A'], 'L0_cond_B': _L0_cond_in['B'], 'L1_cond_W': _L1_cond_in['W'], 'L1_cond_lora_A': _L1_cond_in['lora_A'], 'L1_cond_lora_B': _L1_cond_in['lora_B']}

def reference(x, itok_B_3_7, itok_B_0_15, L0_cond_A, L0_cond_B, L1_cond_W, L1_cond_lora_A, L1_cond_lora_B):
    import jax
    import jax.numpy as jnp

    def _L0_cond_ref(x, A, B, adapter_ids):
        import jax, jax.numpy as jnp
        import numpy as np
        RANK = 16
        ALPHA = 16.0
        SCALING = ALPHA / RANK
        N_ADAPTERS = 8
        IN_F = 2048
        OUT_F = 2048
        BATCH = 4
        SEQ = 1024
        B_sel = B[adapter_ids]
        A_sel = A[adapter_ids]
        Bx = jnp.einsum('bni,bri->bnr', x, B_sel)
        out = jnp.einsum('bnr,bor->bno', Bx, A_sel)
        return out * SCALING

    def _L1_cond_ref(x, adapter_indices, W, lora_A, lora_B):
        import jax, jax.numpy as jnp
        import numpy as np
        SCALING = 16.0 / 16
        base_out = jnp.einsum('bsi,io->bso', x, W)
        A = lora_A[adapter_indices]
        Bm = lora_B[adapter_indices]
        xr = jnp.einsum('bsi,bir->bsr', x, A)
        lora_out = jnp.einsum('bsr,bro->bso', xr, Bm)
        return base_out + lora_out * SCALING
    x = x + _L0_cond_ref(x, L0_cond_A, L0_cond_B, itok_B_3_7)
    x = x + _L1_cond_ref(x, itok_B_0_15, L1_cond_W, L1_cond_lora_A, L1_cond_lora_B)
    return x

_drawn_inputs = setup_inputs


def setup_inputs(seed=0):
    import zlib

    import numpy as np

    out = dict(_drawn_inputs(seed))
    spreads = {}
    factors = {}
    for name, (base, spread) in spreads.items():
        noise = np.random.default_rng([zlib.crc32(name.encode()), seed]).standard_normal(out[name].shape)
        drawn = base * np.exp(spread * noise) if base else spread * noise
        out[name] = jnp.asarray(drawn.astype(out[name].dtype))
    for name, factor in factors.items():
        out[name] = (out[name] * factor).astype(out[name].dtype)
    return out
```

```python
from contextlib import ExitStack

import concourse.bass as bass
from concourse import mybir

F32 = mybir.dt.float32
F32R = mybir.dt.float32r
I32 = mybir.dt.int32
ALU = mybir.AluOpType

P = 128


def lora_residual_program(nc, xT, ids0, ids1, A0, B0, W, A1, B1, yT):
    NB = ids0.shape[1]
    NA0, R, D = A0.shape
    NA1 = B1.shape[0]
    C = D // P
    N = xT.shape[3]
    HALF = C // 2
    REP = P // R
    BANDS = 4
    BAND = P // BANDS
    LEAD = 5

    with ExitStack() as ctx:
        def sb(name, shape, dt=F32):
            return ctx.enter_context(nc.sbuf_tensor(name, shape, dt))

        def pb(name, shape):
            return ctx.enter_context(nc.psum_tensor(name, shape, F32))

        def sem(name):
            return ctx.enter_context(nc.semaphore(name))

        h_hi = [sb(f"h_hi{i}", [P, C, N], F32R) for i in range(2)]
        h_lo = [sb(f"h_lo{i}", [P, C, N], F32R) for i in range(2)]
        w_raw = [sb(f"w_raw{i}", [P, C + 1, P]) for i in range(2)]
        w_hi = [sb(f"w_hi{i}", [P, C + 1, P], F32R) for i in range(2)]
        w_lo = [sb(f"w_lo{i}", [P, C, P], F32R) for i in range(2)]
        xh = [sb(f"xh{i}", [P, 2, N]) for i in range(2)]
        b_raw = sb("b_raw", [P, C, R])
        a1_raw = sb("a1_raw", [P, C, R])
        b_stk = [sb(f"b_stk{i}", [P, 2, BANDS, 2, R], F32R) for i in range(2)]
        a1_stk = [sb(f"a1_stk{i}", [P, 2, BANDS, 2, R], F32R) for i in range(2)]
        a_raw = [sb(f"a_raw{i}", [P, 2 * P]) for i in range(2)]
        a_stk = [sb(f"a_stk{i}", [P, 2 * P], F32R) for i in range(2)]
        bx_stk = sb("bx_stk", [P, N], F32R)
        xr_stk = sb("xr_stk", [P, N], F32R)
        y_out = [sb(f"y_out{i}", [P, N]) for i in range(2)]
        ids = sb("ids", [1, 2, NB], I32)

        y_ps = [pb(f"y_ps{i}", [P, N]) for i in range(2)]
        hd_ps = pb("hd_ps", [P, 2, N])
        bx_ps = pb("bx_ps", [P, N])
        xr_ps = pb("xr_ps", [P, N])

        ids_loaded = sem("ids_loaded")
        w_loaded = [sem(f"w_loaded{i}") for i in range(2)]
        x_loaded = [sem(f"x_loaded{i}") for i in range(2)]
        a_loaded = [sem(f"a_loaded{i}") for i in range(2)]
        b_loaded = sem("b_loaded")
        a1_loaded = sem("a1_loaded")
        y_stored = [sem(f"y_stored{i}") for i in range(2)]
        w_hi_done = sem("w_hi_done")
        w_lo_done = sem("w_lo_done")
        main_done = sem("main_done")
        y_hi_added = sem("y_hi_added")
        y_done = sem("y_done")
        b_hi_done = sem("b_hi_done")
        x_hi_done = sem("x_hi_done")
        a_hi_done = sem("a_hi_done")
        a_lo_done = sem("a_lo_done")
        a1_hi_done = sem("a1_hi_done")
        x_joined = sem("x_joined")
        hd_done = sem("hd_done")
        h_added = sem("h_added")
        h_hi_done = sem("h_hi_done")
        lo_done = sem("lo_done")
        prep_mm_done = sem("prep_mm_done")
        bx_hi_done = sem("bx_hi_done")
        bx_lo_done = sem("bx_lo_done")
        xr_hi_done = sem("xr_hi_done")
        xr_lo_done = sem("xr_lo_done")
        bx_zeroed = sem("bx_zeroed")
        xr_zeroed = sem("xr_zeroed")

        block = ctx.enter_context(nc.Block())

        def two(chunk):
            return bass.ds(chunk, 2)

        @block.sync
        def _(sp):
            sp.dma_start(ids[:, 0, :], ids0).then_inc(ids_loaded, 16)
            sp.dma_start(ids[:, 1, :], ids1).then_inc(ids_loaded, 16)
            sp.wait_ge(ids_loaded, 32)

            def id0(b):
                return sp.value_load(ids[0:1, 0, bass.ds(b, 1)], min_val=0, max_val=NA0 - 1)

            def id1(b):
                return sp.value_load(ids[0:1, 1, bass.ds(b, 1)], min_val=0, max_val=NA1 - 1)

            def rows_rep(dst, src):
                return dst, src.unsqueeze(0).broadcast_to([REP, R, src.shape[-1]])

            def load_w(b, j, u, a1, first=False):
                if not first:
                    sp.wait_ge(w_lo_done, b * C + j - 1)
                sp.dma_start(w_raw[u][:, 0:C, :], W[bass.ds(j, 1), :, :, :].rearrange("a p c n -> (a p) c n")
                             ).then_inc(w_loaded[u], 16)
                dst, src = rows_rep(w_raw[u][:, C, :], B1[bass.ds(a1, 1), :, bass.ds(j * P, P)]
                                    .rearrange("a r n -> (a r) n"))
                sp.dma_start(dst, src).then_inc(w_loaded[u], 16)

            def load_x(bp, j, u, first=False):
                if not first:
                    sp.wait_ge(lo_done, bp * C + j - 1)
                sp.dma_start(xh[u][:, :, :], xT[bass.ds(bp * HALF + j, 1), :, :, :]
                             .rearrange("a p c n -> (a p) c n")).then_inc(x_loaded[u], 16)

            def load_a(bp, k, u, a0, first=False):
                if not first:
                    sp.wait_ge(a_lo_done, bp * HALF + k - 1)
                dst, src = rows_rep(a_raw[u][:, :], A0[bass.ds(a0, 1), :, bass.ds(k * 2 * P, 2 * P)]
                                    .rearrange("a r n -> (a r) n"))
                sp.dma_start(dst, src).then_inc(a_loaded[u], 16)

            def load_b(bp, a0, first=False):
                if not first:
                    sp.wait_ge(lo_done, bp * C - HALF)
                sp.dma_start(b_raw[:, :, :], B0[bass.ds(a0, 1), :, :, :].rearrange("a p c r -> (a p) c r")
                             ).then_inc(b_loaded, 16)

            def load_a1(bp, a1, first=False):
                if not first:
                    sp.wait_ge(lo_done, bp * C)
                sp.dma_start(a1_raw[:, :, :], A1[bass.ds(a1, 1), :, :, :].rearrange("a p c r -> (a p) c r")
                             ).then_inc(a1_loaded, 16)

            def store_y(s, u):
                sp.wait_ge(y_done, s + 1)
                sp.dma_start(yT[bass.ds(s, 1), :, :].rearrange("a p n -> (a p) n"), y_out[u][:, :]
                             ).then_inc(y_stored[u], 16)

            a0, a1 = id0(0), id1(0)
            load_b(0, a0, first=True)
            for u in range(2):
                load_x(0, u, u, first=True)
            load_a1(0, a1, first=True)
            for u in range(2):
                load_a(0, u, u, a0, first=True)
            for u in range(2):
                load_w(0, u, u, a1, first=True)
            with sp.Fori(1, HALF // 2) as jj:
                for u in range(2):
                    load_x(0, 2 * jj + u, u)
            with sp.Fori(1, HALF // 2) as kk:
                for u in range(2):
                    load_a(0, 2 * kk + u, u, a0)

            def batch(b, prep=True, first=False):
                a1_now = id1(b)
                if prep:
                    a0, a1 = id0(b + 1), id1(b + 1)
                    load_b(b + 1, a0)

                def slot(jj, u, kind):
                    j = 2 * jj + u
                    if not (first and isinstance(j, int) and j < 2):
                        load_w(b, j, u, a1_now)
                    if kind == "x":
                        load_x(b + 1, j, u)
                    elif kind == "h":
                        load_a(b + 1, j - HALF, u, a0)
                    if not (first and isinstance(j, int) and j < 3):
                        store_y(b * C + j - 3, 1 - u)

                ahead = 2 if first else 0
                for jj in range(ahead):
                    for u in range(2):
                        slot(jj, u, "x")
                if prep:
                    with sp.Fori(ahead, HALF // 2) as jj:
                        for u in range(2):
                            slot(jj, u, "x")
                    load_a1(b + 1, a1)
                    with sp.Fori(HALF // 2, HALF) as jj:
                        for u in range(2):
                            slot(jj, u, "h")
                else:
                    with sp.Fori(0, HALF) as jj:
                        for u in range(2):
                            slot(jj, u, None)

            batch(0, first=True)
            with sp.Fori(1, NB - 1) as b:
                batch(b)
            batch(NB - 1, prep=False)
            for s in range(NB * C - 3, NB * C):
                store_y(s, s % 2)
            for u in range(2):
                sp.wait_ge(y_stored[u], 16 * (NB * C // 2))

        @block.scalar
        def _(act):
            def split_w(s, u, first=False):
                act.wait_ge(w_loaded[u], (s - u) * 16 + 32)
                if not first:
                    act.wait_ge(main_done, s - 1)
                act.copy(w_hi[u][:, :, :], w_raw[u][:, :, :]).then_inc(w_hi_done, 1)

            def split_cols(stk, raw, k, u, done):
                act.copy(stk[u][:, :, :, 0, :],
                         raw[:, two(k), :].unsqueeze(2).broadcast_to([P, 2, BANDS, R])).then_inc(done, 1)

            def x_step(bp, par, j, u, first=False):
                q = bp * C + j
                act.wait_ge(b_loaded, bp * 16 + 16)
                if not first:
                    act.wait_ge(prep_mm_done, q - 1)
                split_cols(b_stk, b_raw, 2 * j, u, b_hi_done)
                act.wait_ge(x_loaded[u], (bp * HALF + j - u) * 8 + 16)
                act.copy(h_hi[par][:, two(2 * j), :], xh[u][:, :, :]).then_inc(x_hi_done, 1)

            def bx_split(bp):
                act.wait_ge(prep_mm_done, bp * C + HALF)
                act.copy(bx_stk[:, :], bx_ps[:, :]).then_inc(bx_hi_done, 1)

            def h_step(bp, par, j, u):
                q, k = bp * C + j, j - HALF
                act.wait_ge(a_loaded[u], (bp * HALF + k - u) * 8 + 16)
                act.wait_ge(prep_mm_done, q - 1)
                act.copy(a_stk[u][:, :], a_raw[u][:, :]).then_inc(a_hi_done, 1)
                act.wait_ge(a1_loaded, bp * 16 + 16)
                split_cols(a1_stk, a1_raw, 2 * k, u, a1_hi_done)
                act.wait_ge(h_added, bp * HALF + k + 1)
                act.copy(h_hi[par][:, two(2 * k), :], xh[u][:, :, :]).then_inc(h_hi_done, 1)

            def xr_split(b):
                act.wait_ge(prep_mm_done, b * C + C)
                act.wait_ge(main_done, b * C)
                act.copy(xr_stk[:, :], xr_ps[:, :]).then_inc(xr_hi_done, 1)

            for u in range(2):
                x_step(0, 0, u, u, first=True)
            split_w(0, 0, first=True)
            with act.Fori(1, HALF // 2) as jj:
                for u in range(2):
                    x_step(0, 0, 2 * jj + u, u)
            bx_split(0)
            with act.Fori(HALF // 2, HALF) as jj:
                for u in range(2):
                    h_step(0, 0, 2 * jj + u, u)

            def batch(b, par, prep=True):
                xr_split(b)
                if prep:
                    act.wait_ge(y_done, b * C)
                    with act.Fori(0, HALF // 2) as jj:
                        for u in range(2):
                            j = 2 * jj + u
                            split_w(b * C + j + 1, 1 - u)
                            x_step(b + 1, 1 - par, j, u)
                    bx_split(b + 1)
                    with act.Fori(HALF // 2, HALF) as jj:
                        for u in range(2):
                            j = 2 * jj + u
                            split_w(b * C + j + 1, 1 - u)
                            h_step(b + 1, 1 - par, j, u)
                else:
                    split_w(b * C + 1, 1)
                    with act.Fori(1, HALF) as jj:
                        for u in range(2):
                            split_w(b * C + 2 * jj + u, u)

            with act.Fori(0, NB // 2 - 1) as pair:
                for par in range(2):
                    batch(2 * pair + par, par)
            batch(NB - 2, 0)
            batch(NB - 1, 1, prep=False)

        @block.vector
        def _(dve):
            def split_w(s, u):
                dve.wait_ge(w_hi_done, s + 1)
                dve.tensor_tensor(w_hi[u][P // 2:P, C, :], w_raw[u][P // 2:P, C, :],
                                  w_hi[u][P // 2:P, C, :].bitcast(F32), ALU.subtract)
                dve.tensor_tensor(w_lo[u][:, :, :], w_raw[u][:, 0:C, :],
                                  w_hi[u][:, 0:C, :].bitcast(F32), ALU.subtract).then_inc(w_lo_done, 1)

            def split_cols(stk, raw, k, u):
                dve.tensor_tensor(stk[u][:, :, :, 1, :],
                                  raw[:, two(k), :].unsqueeze(2).broadcast_to([P, 2, BANDS, R]),
                                  stk[u][:, :, :, 0, :].bitcast(F32), ALU.subtract)

            def split_bands(b, stk, ps, done, zeroed):
                for band in (1, 3):
                    rows = slice(band * BAND, (band + 1) * BAND)
                    last = dve.tensor_tensor(stk[rows, :], ps[rows, :], stk[rows, :].bitcast(F32), ALU.subtract)
                last.then_inc(done, 1)
                dve.wait_ge(done, b + 1)
                dve.memset(ps[:, :], 0.0).then_inc(zeroed, 1)

            def x_step(bp, par, j, u):
                dve.wait_ge(b_hi_done, bp * HALF + j + 1)
                split_cols(b_stk, b_raw, 2 * j, u)
                dve.wait_ge(x_hi_done, bp * HALF + j + 1)
                dve.tensor_tensor(h_lo[par][:, two(2 * j), :], xh[u][:, :, :],
                                  h_hi[par][:, two(2 * j), :].bitcast(F32), ALU.subtract).then_inc(lo_done, 1)

            def bx_split(bp):
                dve.wait_ge(bx_hi_done, bp + 1)
                split_bands(bp, bx_stk, bx_ps, bx_lo_done, bx_zeroed)

            def h_step(bp, par, j, u):
                k = j - HALF
                n = bp * HALF + k
                dve.wait_ge(lo_done, bp * C + HALF)
                dve.tensor_tensor(xh[u][:, :, :], h_hi[par][:, two(2 * k), :].bitcast(F32),
                                  h_lo[par][:, two(2 * k), :].bitcast(F32), ALU.add).then_inc(x_joined, 1)
                dve.wait_ge(a_hi_done, n + 1)
                dve.tensor_tensor(a_stk[u][P // 2:P, :], a_raw[u][P // 2:P, :],
                                  a_stk[u][P // 2:P, :].bitcast(F32), ALU.subtract).then_inc(a_lo_done, 1)
                dve.wait_ge(a1_hi_done, n + 1)
                split_cols(a1_stk, a1_raw, 2 * k, u)
                dve.wait_ge(x_joined, n + 1)
                dve.wait_ge(hd_done, n + 1)
                dve.tensor_tensor(xh[u][:, :, :], hd_ps[:, :, :], xh[u][:, :, :], ALU.add).then_inc(h_added, 1)
                dve.wait_ge(h_hi_done, n + 1)
                dve.tensor_tensor(h_lo[par][:, two(2 * k), :], xh[u][:, :, :],
                                  h_hi[par][:, two(2 * k), :].bitcast(F32), ALU.subtract).then_inc(lo_done, 1)

            def xr_split(b):
                dve.wait_ge(xr_hi_done, b + 1)
                split_bands(b, xr_stk, xr_ps, xr_lo_done, xr_zeroed)

            def finish_y(b, par, j, u):
                s = b * C + j
                dve.wait_ge(main_done, s + 1)
                dve.wait_ge(y_stored[u], (s - u) * 8)
                one = bass.ds(j, 1)
                dve.tensor_tensor(y_out[u][:, :], y_ps[u][:, :],
                                  h_hi[par][:, one, :].rearrange("p a n -> p (a n)").bitcast(F32),
                                  ALU.add).then_inc(y_hi_added, 1)
                dve.wait_ge(y_hi_added, s + 1)
                dve.tensor_tensor(y_out[u][:, :], y_out[u][:, :],
                                  h_lo[par][:, one, :].rearrange("p a n -> p (a n)").bitcast(F32),
                                  ALU.add).then_inc(y_done, 1)

            dve.memset(bx_ps[:, :], 0.0).then_inc(bx_zeroed, 1)
            dve.memset(xr_ps[:, :], 0.0).then_inc(xr_zeroed, 1)
            for u in range(2):
                x_step(0, 0, u, u)
            split_w(0, 0)
            with dve.Fori(1, HALF // 2) as jj:
                for u in range(2):
                    x_step(0, 0, 2 * jj + u, u)
            bx_split(0)
            with dve.Fori(HALF // 2, HALF) as jj:
                for u in range(2):
                    h_step(0, 0, 2 * jj + u, u)

            def batch(b, par, prep=True):
                xr_split(b)
                if prep:
                    with dve.Fori(0, HALF // 2) as jj:
                        for u in range(2):
                            j = 2 * jj + u
                            split_w(b * C + j + 1, 1 - u)
                            x_step(b + 1, 1 - par, j, u)
                            finish_y(b, par, j, u)
                    bx_split(b + 1)
                    with dve.Fori(HALF // 2, HALF) as jj:
                        for u in range(2):
                            j = 2 * jj + u
                            split_w(b * C + j + 1, 1 - u)
                            h_step(b + 1, 1 - par, j, u)
                            finish_y(b, par, j, u)
                else:
                    with dve.Fori(0, HALF - 1) as jj:
                        for u in range(2):
                            j = 2 * jj + u
                            split_w(b * C + j + 1, 1 - u)
                            finish_y(b, par, j, u)
                    split_w(b * C + C - 1, 1)
                    for j in range(C - 2, C):
                        finish_y(b, par, j, j % 2)

            with dve.Fori(0, NB // 2 - 1) as pair:
                for par in range(2):
                    batch(2 * pair + par, par)
            batch(NB - 2, 0)
            batch(NB - 1, 1, prep=False)

        @block.tensor
        def _(pe):
            def bx_chunks(bp, par, j, u):
                pe.wait_ge(bx_zeroed, bp + 1)
                pe.wait_ge(lo_done, bp * C + j + 1)
                accumulate(bx_ps, b_stk, par, 2 * j, u)

            def xr_chunks(bp, par, j, u):
                pe.wait_ge(xr_zeroed, bp + 1)
                pe.wait_ge(lo_done, bp * C + j + 1)
                accumulate(xr_ps, a1_stk, par, 2 * (j - HALF), u)

            def accumulate(ps, stk, par, c0, u):
                for c in range(2):
                    cols = stk[u][:, c, :, :, :].rearrange("p a b r -> p (a b r)")
                    for h in (h_hi[par], h_lo[par]):
                        last = pe.matmul(ps[:, :], cols,
                                         h[:, bass.ds(c0 + c, 1), :].rearrange("p a n -> p (a n)"),
                                         start=False, stop=False, skip_group_check=True)
                last.then_inc(prep_mm_done, 1)

            def h_delta(bp, j, u):
                n = bp * HALF + j - HALF
                pe.wait_ge(bx_lo_done, bp + 1)
                pe.wait_ge(a_lo_done, n + 1)
                pe.wait_ge(h_added, n)
                for c in range(2):
                    last = pe.matmul(hd_ps[:, c, :], a_stk[u][:, c * P:(c + 1) * P], bx_stk[:, :],
                                     start=True, stop=True)
                last.then_inc(hd_done, 1)

            def main(b, par, j, u, chunks):
                for c in chunks:
                    if c == 0:
                        pe.wait_ge(w_lo_done, b * C + j + 1)
                    for w, h in ((w_hi, h_hi), (w_hi, h_lo), (w_lo, h_hi)):
                        pe.matmul(y_ps[u][:, :], w[u][:, c, :], h[par][:, c, :],
                                  start=(c == 0 and w is w_hi and h is h_hi), stop=False)

            def low_rank_out(b, u):
                pe.wait_ge(xr_lo_done, b + 1)
                pe.matmul(y_ps[u][:, :], w_hi[u][:, C, :], xr_stk[:, :], start=False, stop=True
                          ).then_inc(main_done, 1)

            def batch(b, par, prep=True):
                if prep:
                    for jj0, jj1, kind in ((0, HALF // 2, "x"), (HALF // 2, HALF, "h")):
                        with pe.Fori(jj0, jj1) as jj:
                            for u in range(2):
                                j = 2 * jj + u
                                if kind == "x":
                                    main(b, par, j, u, range(C))
                                    low_rank_out(b, u)
                                    bx_chunks(b + 1, 1 - par, j, u)
                                else:
                                    main(b, par, j, u, range(LEAD))
                                    h_delta(b + 1, j, u)
                                    main(b, par, j, u, range(LEAD, C))
                                    low_rank_out(b, u)
                                    xr_chunks(b + 1, 1 - par, j, u)
                else:
                    with pe.Fori(0, HALF) as jj:
                        for u in range(2):
                            main(b, par, 2 * jj + u, u, range(C))
                            low_rank_out(b, u)

            with pe.Fori(0, HALF // 2) as jj:
                for u in range(2):
                    bx_chunks(0, 0, 2 * jj + u, u)
            with pe.Fori(HALF // 2, HALF) as jj:
                for u in range(2):
                    h_delta(0, 2 * jj + u, u)
                    xr_chunks(0, 0, 2 * jj + u, u)
            with pe.Fori(0, NB // 2 - 1) as pair:
                for par in range(2):
                    batch(2 * pair + par, par)
            batch(NB - 2, 0)
            batch(NB - 1, 1, prep=False)


_INS = ["xT", "ids0", "ids1", "A0", "B0", "W", "A1", "B1"]


def kernel(x, itok_B_3_7, itok_B_0_15, L0_cond_A, L0_cond_B, L1_cond_W, L1_cond_lora_A, L1_cond_lora_B):
    import numpy as np
    import concourse.bacc as bacc
    from concourse.bass_utils import run_bass_kernel_spmd

    nb, n, d = x.shape
    c = d // P
    a0, b0, w, a1, b1 = (np.asarray(v) for v in (L0_cond_A, L0_cond_B, L1_cond_W, L1_cond_lora_A,
                                                 L1_cond_lora_B))
    r = a0.shape[2]
    laid = {
        "xT": np.asarray(x).transpose(0, 2, 1).reshape(nb, c // 2, 2, P, n).transpose(0, 1, 3, 2, 4)
                           .reshape(nb * c // 2, P, 2, n),
        "ids0": np.asarray(itok_B_3_7).reshape(1, nb),
        "ids1": np.asarray(itok_B_0_15).reshape(1, nb),
        "A0": a0.transpose(0, 2, 1),
        "B0": b0.reshape(-1, r, c, P).transpose(0, 3, 2, 1),
        "W": w.reshape(c, P, c, P).transpose(2, 1, 0, 3),
        "A1": a1.reshape(-1, c, P, r).transpose(0, 2, 1, 3),
        "B1": b1,
    }
    nc = bacc.Bacc("TRN2", target_bir_lowering=False, num_devices=1)
    arrays, args = {}, []
    for name in _INS:
        a = np.ascontiguousarray(laid[name])
        arrays[f"in_{name}"] = a
        args.append(nc.dram_tensor(f"in_{name}", a.shape, mybir.dt.from_np(a.dtype), kind="ExternalInput").ap())
    out = nc.dram_tensor("out_y", (nb * c, P, n), F32, kind="ExternalOutput").ap()
    lora_residual_program(nc, *args, out)
    got = run_bass_kernel_spmd(nc, [arrays], core_ids=[0]).results[0]["out_y"]
    return np.ascontiguousarray(got.reshape(nb, d, n).transpose(0, 2, 1))
```

```python
from contextlib import ExitStack

import concourse.bass as bass
from concourse import mybir

F32 = mybir.dt.float32
F32R = mybir.dt.float32r
I32 = mybir.dt.int32
ALU = mybir.AluOpType

P = 128


def lora_residual_program(nc, xT, ids0, ids1, A0, A0n, B0, W, A1, B1, yT):
    NB = ids0.shape[1]
    NA0, R, D = A0.shape
    NA1 = B1.shape[0]
    C = D // P
    N = xT.shape[3]
    HALF = C // 2
    REP = P // R
    BANDS = 4
    BAND = P // BANDS
    LEAD = 9

    with ExitStack() as ctx:
        def sb(name, shape, dt=F32):
            return ctx.enter_context(nc.sbuf_tensor(name, shape, dt))

        def pb(name, shape):
            return ctx.enter_context(nc.psum_tensor(name, shape, F32))

        def sem(name):
            return ctx.enter_context(nc.semaphore(name))

        h_hi = [sb(f"h_hi{i}", [P, C, N], F32R) for i in range(2)]
        h_lo = [sb(f"h_lo{i}", [P, C, N], F32R) for i in range(2)]
        w_raw = [sb(f"w_raw{i}", [P, C + 1, P]) for i in range(2)]
        w_hi = [sb(f"w_hi{i}", [P, C + 1, P], F32R) for i in range(2)]
        w_lo = [sb(f"w_lo{i}", [P, C, P], F32R) for i in range(2)]
        xh = [sb(f"xh{i}", [P, 2, N]) for i in range(2)]
        b_raw = sb("b_raw", [P, C, R])
        a1_raw = sb("a1_raw", [P, C, R])
        a0_raw = sb("a0_raw", [P, C, R])
        lr_stk = [sb(f"lr_stk{i}", [P, 2, 2, 2, 2, R], F32R) for i in range(2)]
        a0_stk = [sb(f"a0_stk{i}", [P, 2, REP, R], F32R) for i in range(2)]
        g_hi = sb("g_hi", [P, 2, 2, 2, R], F32R)
        g_lo = sb("g_lo", [P, 2, 2, 2, R], F32R)
        a_raw = [sb(f"a_raw{i}", [P, 2 * P]) for i in range(2)]
        a_stk = [sb(f"a_stk{i}", [P, 2 * P], F32R) for i in range(2)]
        bx_stk = sb("bx_stk", [P, N], F32R)
        xr_stk = sb("xr_stk", [P, N], F32R)
        y_out = [sb(f"y_out{i}", [P, N]) for i in range(2)]
        ids = sb("ids", [1, 2, NB], I32)

        y_ps = [pb(f"y_ps{i}", [P, N]) for i in range(2)]
        hd_ps = pb("hd_ps", [P, 2, N])
        lr_ps = pb("lr_ps", [P, N])
        g_ps = pb("g_ps", [P, 2 * R])

        ids_loaded = sem("ids_loaded")
        w_loaded = [sem(f"w_loaded{i}") for i in range(2)]
        x0_loaded = [sem(f"x0_loaded{i}") for i in range(4)]
        x_loaded = [sem(f"x_loaded{i}") for i in range(2)]
        a_loaded = [sem(f"a_loaded{i}") for i in range(2)]
        b_loaded = sem("b_loaded")
        a1_loaded = sem("a1_loaded")
        a0_loaded = sem("a0_loaded")
        y_stored = [sem(f"y_stored{i}") for i in range(2)]
        w_hi_done = sem("w_hi_done")
        w_lo_done = sem("w_lo_done")
        main_done = sem("main_done")
        y_hi_added = sem("y_hi_added")
        y_done = sem("y_done")
        lr_hi_done = sem("lr_hi_done")
        x0_hi_done = sem("x0_hi_done")
        x0_lo_done = sem("x0_lo_done")
        x_hi_done = sem("x_hi_done")
        prep_mm_done = sem("prep_mm_done")
        a_hi_done = sem("a_hi_done")
        a_lo_done = sem("a_lo_done")
        x_joined = sem("x_joined")
        hd_done = sem("hd_done")
        h_added = sem("h_added")
        h_hi_done = sem("h_hi_done")
        lo_done = sem("lo_done")
        g_hi_done = sem("g_hi_done")
        g_lo_done = sem("g_lo_done")
        bx_hi_done = sem("bx_hi_done")
        bx_lo_done = sem("bx_lo_done")
        bx_done = sem("bx_done")
        xr_done = sem("xr_done")
        xr_hi_done = sem("xr_hi_done")
        xr_lo_done = sem("xr_lo_done")
        xr_stacked = sem("xr_stacked")
        lr_zeroed = sem("lr_zeroed")

        block = ctx.enter_context(nc.Block())

        def two(chunk):
            return bass.ds(chunk, 2)

        @block.sync
        def _(sp):
            sp.dma_start(ids[:, 0, :], ids0).then_inc(ids_loaded, 16)
            sp.dma_start(ids[:, 1, :], ids1).then_inc(ids_loaded, 16)
            sp.wait_ge(ids_loaded, 32)

            def id0(b):
                return sp.value_load(ids[0:1, 0, bass.ds(b, 1)], min_val=0, max_val=NA0 - 1)

            def id1(b):
                return sp.value_load(ids[0:1, 1, bass.ds(b, 1)], min_val=0, max_val=NA1 - 1)

            def rows_rep(dst, src):
                return dst, src.unsqueeze(0).broadcast_to([REP, R, src.shape[-1]])

            def load_w(b, j, u, a1, first=False):
                if not first:
                    sp.wait_ge(w_lo_done, b * C + j - 1)
                sp.dma_start(w_raw[u][:, 0:C, :], W[bass.ds(j, 1), :, :, :].rearrange("a p c n -> (a p) c n")
                             ).then_inc(w_loaded[u], 16)
                dst, src = rows_rep(w_raw[u][:, C, :], B1[bass.ds(a1, 1), :, bass.ds(j * P, P)]
                                    .rearrange("a r n -> (a r) n"))
                sp.dma_start(dst, src).then_inc(w_loaded[u], 16)

            def load_x0(jj, first=False):
                for u in range(2):
                    for c in range(2):
                        if not first:
                            sp.wait_ge((x0_lo_done, lo_done)[c], 2 * jj + u - 1)
                        sp.dma_start(xh[u][:, c, :], xT[bass.ds(2 * jj + u, 1), :, c, :]
                                     .rearrange("a p n -> (a p) n")).then_inc(x0_loaded[2 * u + c], 16)

            def load_x(bp, j, u):
                sp.wait_ge(lo_done, bp * C + j - 1)
                sp.dma_start(xh[u][:, :, :], xT[bass.ds(bp * HALF + j, 1), :, :, :]
                             .rearrange("a p c n -> (a p) c n")).then_inc(x_loaded[u], 16)

            def load_a(bp, k, u, a0, first=False):
                if not first:
                    sp.wait_ge(a_lo_done, bp * HALF + k - 1)
                dst, src = rows_rep(a_raw[u][:, :], A0[bass.ds(a0, 1), :, bass.ds(k * 2 * P, 2 * P)]
                                    .rearrange("a r n -> (a r) n"))
                sp.dma_start(dst, src).then_inc(a_loaded[u], 16)

            def load_low_rank(bp, a0, a1, first=False):
                if not first:
                    sp.wait_ge(prep_mm_done, bp * HALF)
                for dst, src, a, loaded in ((b_raw, B0, a0, b_loaded), (a1_raw, A1, a1, a1_loaded),
                                            (a0_raw, A0n, a0, a0_loaded)):
                    sp.dma_start(dst[:, :, :], src[bass.ds(a, 1), :, :, :].rearrange("a p c r -> (a p) c r")
                                 ).then_inc(loaded, 16)

            def store_y(s, u):
                sp.wait_ge(y_done, s + 1)
                sp.dma_start(yT[bass.ds(s, 1), :, :].rearrange("a p n -> (a p) n"), y_out[u][:, :]
                             ).then_inc(y_stored[u], 16)

            for u in range(2):
                sp.sem_inc(y_stored[u], 1)
            a0, a1 = id0(0), id1(0)
            load_low_rank(0, a0, a1, first=True)
            load_x0(0, first=True)
            load_x0(1)
            load_w(0, 0, 0, a1, first=True)
            with sp.Fori(2, HALF // 2) as jj:
                load_x0(jj)
            for u in range(2):
                load_a(0, u, u, a0, first=True)
            load_w(0, 1, 1, a1, first=True)
            load_w(0, 2, 0, a1)
            for u in range(2):
                load_a(0, 2 + u, u, a0)
            load_w(0, 3, 1, a1)
            with sp.Fori(2, HALF // 2) as kk:
                for u in range(2):
                    load_a(0, 2 * kk + u, u, a0)

            def batch(b, prep=True, first=False):
                a1_now = id1(b)
                if prep:
                    a0, a1 = id0(b + 1), id1(b + 1)
                    load_low_rank(b + 1, a0, a1)

                def slot(jj, u, kind):
                    j = 2 * jj + u
                    if not (first and isinstance(j, int) and j < 4):
                        load_w(b, j, u, a1_now)
                    if kind == "x":
                        load_x(b + 1, j, u)
                    elif kind == "h":
                        load_a(b + 1, j - HALF, u, a0)
                    if not (first and isinstance(j, int) and j < 3):
                        store_y(b * C + j - 3, 1 - u)

                ahead = 2 if first else 0
                for jj in range(ahead):
                    for u in range(2):
                        slot(jj, u, "x")
                if prep:
                    with sp.Fori(ahead, HALF // 2) as jj:
                        for u in range(2):
                            slot(jj, u, "x")
                    with sp.Fori(HALF // 2, HALF) as jj:
                        for u in range(2):
                            slot(jj, u, "h")
                else:
                    with sp.Fori(0, HALF) as jj:
                        for u in range(2):
                            slot(jj, u, None)

            batch(0, first=True)
            with sp.Fori(1, NB - 1) as b:
                batch(b)
            batch(NB - 1, prep=False)
            for s in range(NB * C - 3, NB * C):
                store_y(s, s % 2)
            for u in range(2):
                sp.wait_ge(y_stored[u], 16 * (NB * C // 2) + 1)

        @block.scalar
        def _(act):
            def split_w(s, u, first=False):
                act.wait_ge(w_loaded[u], (s - u) * 16 + 32)
                if not first:
                    act.wait_ge(main_done, s)
                act.copy(w_hi[u][:, :, :], w_raw[u][:, :, :]).then_inc(w_hi_done, 1)

            def low_rank_split(bp, j, u, first=False):
                if not first:
                    act.wait_ge(prep_mm_done, bp * HALF + j - 1)
                for which, (raw, loaded) in enumerate(((b_raw, b_loaded), (a1_raw, a1_loaded))):
                    act.wait_ge(loaded, bp * 16 + 16)
                    act.copy(lr_stk[u][:, :, which, :, 0, :],
                             raw[:, two(2 * j), :].unsqueeze(2).broadcast_to([P, 2, 2, R]))
                act.wait_ge(a0_loaded, bp * 16 + 16)
                act.copy(a0_stk[u][:, :, :, :],
                         a0_raw[:, two(2 * j), :].unsqueeze(2).broadcast_to([P, 2, REP, R])
                         ).then_inc(lr_hi_done, 1)

            def x0_steps(jj, first=False):
                for u in range(2):
                    j = 2 * jj + u
                    low_rank_split(0, j, u, first=first)
                    for c in range(2):
                        act.wait_ge(x0_loaded[2 * u + c], jj * 16 + 16)
                        act.copy(h_hi[0][:, bass.ds(2 * j + c, 1), :].rearrange("p a n -> p (a n)"),
                                 xh[u][:, c, :]).then_inc(x0_hi_done, 1)

            def x_step(bp, par, j, u):
                low_rank_split(bp, j, u)
                act.wait_ge(x_loaded[u], ((bp - 1) * HALF + j - u) * 8 + 16)
                act.copy(h_hi[par][:, two(2 * j), :], xh[u][:, :, :]).then_inc(x_hi_done, 1)

            def bx_split(bp):
                act.wait_ge(prep_mm_done, (bp + 1) * HALF)
                act.copy(bx_stk[0:P // 2, :], lr_ps[0:P // 2, :]).then_inc(bx_hi_done, 1)
                act.copy(g_hi[:, 1, :, :, :].rearrange("p d s r -> p d (s r)"),
                         g_ps[:, :].unsqueeze(1).broadcast_to([P, 2, 2 * R])).then_inc(g_hi_done, 1)
                act.wait_ge(bx_lo_done, bp + 1)
                act.copy(bx_stk[P // 2:P, :], bx_stk[0:P // 2, :].bitcast(F32)).then_inc(bx_done, 1)

            def a_split(bp, j, u, first=False):
                n = bp * HALF + j - HALF
                act.wait_ge(a_loaded[u], (n - u) * 8 + 16)
                if not first:
                    act.wait_ge(hd_done, n - 1)
                act.copy(a_stk[u][:, :], a_raw[u][:, :]).then_inc(a_hi_done, 1)

            def h_split(bp, par, j, u):
                k = j - HALF
                act.wait_ge(h_added, bp * HALF + k + 1)
                act.copy(h_hi[par][:, two(2 * k), :], xh[u][:, :, :]).then_inc(h_hi_done, 1)

            def xr_split(b):
                act.wait_ge(xr_done, b + 1)
                act.copy(xr_stk[P // 2:P, :], lr_ps[P // 2:P, :]).then_inc(xr_hi_done, 1)
                act.wait_ge(xr_lo_done, b + 1)
                act.copy(xr_stk[0:P // 2, :], xr_stk[P // 2:P, :].bitcast(F32)).then_inc(xr_stacked, 1)

            x0_steps(0, first=True)
            with act.Fori(1, HALF // 2 - 1) as jj:
                x0_steps(jj)
            split_w(0, 0, first=True)
            x0_steps(HALF // 2 - 1)
            a_split(0, HALF, 0, first=True)
            a_split(0, HALF + 1, 1, first=True)
            bx_split(0)
            h_split(0, 0, HALF, 0)
            split_w(1, 1, first=True)
            a_split(0, HALF + 2, 0)
            h_split(0, 0, HALF + 1, 1)
            xr_split(0)
            with act.Fori(HALF // 2 + 1, HALF - 1) as jj:
                for u in range(2):
                    a_split(0, 2 * jj + u + 1, 1 - u)
                    h_split(0, 0, 2 * jj + u, u)
            a_split(0, C - 1, 1)
            for u in range(2):
                h_split(0, 0, C - 2 + u, u)

            def batch(b, par, prep=True, first=False):
                def x_slot(j, u, w_split=True):
                    if w_split:
                        split_w(b * C + j + 1, 1 - u)
                    x_step(b + 1, 1 - par, j, u)

                if not first:
                    xr_split(b)
                    if prep:
                        act.wait_ge(xr_lo_done, b + 1)
                if not prep:
                    split_w(b * C + 1, 1)
                    with act.Fori(1, HALF) as jj:
                        for u in range(2):
                            split_w(b * C + 2 * jj + u, u)
                    return
                if first:
                    x_slot(0, 0, w_split=False)
                    x_slot(1, 1)
                with act.Fori(1 if first else 0, HALF // 2) as jj:
                    for u in range(2):
                        x_slot(2 * jj + u, u)
                bx_split(b + 1)
                with act.Fori(HALF // 2, HALF) as jj:
                    for u in range(2):
                        j = 2 * jj + u
                        a_split(b + 1, j, u)
                        split_w(b * C + j + 1, 1 - u)
                        h_split(b + 1, 1 - par, j, u)

            batch(0, 0, first=True)
            batch(1, 1)
            with act.Fori(1, NB // 2 - 1) as pair:
                for par in range(2):
                    batch(2 * pair + par, par)
            batch(NB - 2, 0)
            batch(NB - 1, 1, prep=False)

        @block.vector
        def _(dve):
            def split_w(s, u):
                dve.wait_ge(w_hi_done, s + 1)
                dve.tensor_tensor(w_hi[u][P // 2:P, C, :], w_raw[u][P // 2:P, C, :],
                                  w_hi[u][P // 2:P, C, :].bitcast(F32), ALU.subtract)
                dve.tensor_tensor(w_lo[u][:, :, :], w_raw[u][:, 0:C, :],
                                  w_hi[u][:, 0:C, :].bitcast(F32), ALU.subtract).then_inc(w_lo_done, 1)

            def low_rank_split(bp, j, u):
                dve.wait_ge(lr_hi_done, bp * HALF + j + 1)
                for which, raw in enumerate((b_raw, a1_raw)):
                    dve.tensor_tensor(lr_stk[u][:, :, which, :, 1, :],
                                      raw[:, two(2 * j), :].unsqueeze(2).broadcast_to([P, 2, 2, R]),
                                      lr_stk[u][:, :, which, :, 0, :].bitcast(F32), ALU.subtract)
                dve.tensor_tensor(a0_stk[u][:, :, REP // 2:REP, :],
                                  a0_raw[:, two(2 * j), :].unsqueeze(2).broadcast_to([P, 2, REP // 2, R]),
                                  a0_stk[u][:, :, REP // 2:REP, :].bitcast(F32), ALU.subtract)

            def x0_steps(jj):
                for u in range(2):
                    j = 2 * jj + u
                    low_rank_split(0, j, u)
                    for c in range(2):
                        one = bass.ds(2 * j + c, 1)
                        dve.wait_ge(x0_hi_done, 2 * j + c + 1)
                        dve.tensor_tensor(h_lo[0][:, one, :].rearrange("p a n -> p (a n)"), xh[u][:, c, :],
                                          h_hi[0][:, one, :].rearrange("p a n -> p (a n)").bitcast(F32),
                                          ALU.subtract).then_inc((x0_lo_done, lo_done)[c], 1)

            def x_step(bp, par, j, u):
                low_rank_split(bp, j, u)
                dve.wait_ge(x_hi_done, (bp - 1) * HALF + j + 1)
                dve.tensor_tensor(h_lo[par][:, two(2 * j), :], xh[u][:, :, :],
                                  h_hi[par][:, two(2 * j), :].bitcast(F32), ALU.subtract).then_inc(lo_done, 1)

            def bx_split(bp):
                dve.wait_ge(bx_hi_done, bp + 1)
                dve.tensor_tensor(bx_stk[BAND:2 * BAND, :], lr_ps[BAND:2 * BAND, :],
                                  bx_stk[BAND:2 * BAND, :].bitcast(F32), ALU.subtract).then_inc(bx_lo_done, 1)
                dve.wait_ge(g_hi_done, bp + 1)
                dve.tensor_tensor(g_lo[:, 1, :, :, :].rearrange("p d s r -> p d (s r)"),
                                  g_ps[:, :].unsqueeze(1).broadcast_to([P, 2, 2 * R]),
                                  g_hi[:, 1, :, :, :].rearrange("p d s r -> p d (s r)").bitcast(F32),
                                  ALU.subtract).then_inc(g_lo_done, 1)
                dve.wait_ge(g_lo_done, bp + 1)
                dve.memset(g_ps[:, :], 0.0)

            def join_x(bp, par, j, u):
                k = j - HALF
                dve.wait_ge(lo_done, bp * C + HALF)
                dve.wait_ge(lo_done, bp * C + j - 1)
                dve.tensor_tensor(xh[u][:, :, :], h_hi[par][:, two(2 * k), :].bitcast(F32),
                                  h_lo[par][:, two(2 * k), :].bitcast(F32), ALU.add).then_inc(x_joined, 1)

            def a_split(bp, j, u):
                dve.wait_ge(a_hi_done, bp * HALF + j - HALF + 1)
                dve.tensor_tensor(a_stk[u][P // 2:P, :], a_raw[u][P // 2:P, :],
                                  a_stk[u][P // 2:P, :].bitcast(F32), ALU.subtract).then_inc(a_lo_done, 1)

            def add_delta(bp, j, u):
                n = bp * HALF + j - HALF
                dve.wait_ge(x_joined, n + 1)
                dve.wait_ge(hd_done, n + 1)
                dve.tensor_tensor(xh[u][:, :, :], hd_ps[:, :, :], xh[u][:, :, :], ALU.add).then_inc(h_added, 1)

            def h_split(bp, par, j, u):
                k = j - HALF
                n = bp * HALF + k
                dve.wait_ge(h_hi_done, n + 1)
                dve.tensor_tensor(h_lo[par][:, two(2 * k), :], xh[u][:, :, :],
                                  h_hi[par][:, two(2 * k), :].bitcast(F32), ALU.subtract).then_inc(lo_done, 1)

            def xr_split(b):
                dve.wait_ge(xr_hi_done, b + 1)
                dve.tensor_tensor(xr_stk[3 * BAND:P, :], lr_ps[3 * BAND:P, :],
                                  xr_stk[3 * BAND:P, :].bitcast(F32), ALU.subtract).then_inc(xr_lo_done, 1)
                dve.wait_ge(xr_lo_done, b + 1)
                dve.memset(lr_ps[:, :], 0.0).then_inc(lr_zeroed, 1)

            def finish_y(b, par, j, u):
                s = b * C + j
                dve.wait_ge(main_done, s + 2)
                dve.wait_ge(y_stored[u], (s - u) * 8 + 1)
                one = bass.ds(j, 1)
                dve.tensor_tensor(y_out[u][:, :], y_ps[u][:, :],
                                  h_hi[par][:, one, :].rearrange("p a n -> p (a n)").bitcast(F32),
                                  ALU.add).then_inc(y_hi_added, 1)
                dve.wait_ge(y_hi_added, s + 1)
                dve.tensor_tensor(y_out[u][:, :], y_out[u][:, :],
                                  h_lo[par][:, one, :].rearrange("p a n -> p (a n)").bitcast(F32),
                                  ALU.add).then_inc(y_done, 1)

            dve.memset(g_ps[:, :], 0.0)
            dve.memset(lr_ps[:, :], 0.0).then_inc(lr_zeroed, 1)
            dve.memset(g_hi[:, 0, :, :, :].bitcast(F32), 0.0)
            dve.memset(g_lo[:, 0, :, :, :].bitcast(F32), 0.0)

            def h0_step(j, u, ahead=True):
                add_delta(0, j, u)
                if ahead:
                    a_split(0, j + 1, 1 - u)
                    join_x(0, 0, j + 1, 1 - u)
                h_split(0, 0, j, u)

            x0_steps(0)
            with dve.Fori(1, HALF // 2 - 1) as jj:
                x0_steps(jj)
            split_w(0, 0)
            x0_steps(HALF // 2 - 1)
            a_split(0, HALF, 0)
            join_x(0, 0, HALF, 0)
            bx_split(0)
            h0_step(HALF, 0)
            split_w(1, 1)
            h0_step(HALF + 1, 1)
            xr_split(0)
            with dve.Fori(HALF // 2 + 1, HALF - 1) as jj:
                for u in range(2):
                    h0_step(2 * jj + u, u)
            h0_step(C - 2, 0)
            h0_step(C - 1, 1, ahead=False)

            def batch(b, par, prep=True, first=False):
                def x_slot(j, u, w_split=True):
                    if w_split:
                        split_w(b * C + j + 1, 1 - u)
                    x_step(b + 1, 1 - par, j, u)
                    finish_y(b, par, j, u)

                if not first:
                    xr_split(b)
                if not prep:
                    with dve.Fori(0, HALF - 1) as jj:
                        for u in range(2):
                            j = 2 * jj + u
                            split_w(b * C + j + 1, 1 - u)
                            finish_y(b, par, j, u)
                    split_w(b * C + C - 1, 1)
                    for j in range(C - 2, C):
                        finish_y(b, par, j, j % 2)
                    return
                if first:
                    x_slot(0, 0, w_split=False)
                    x_slot(1, 1)
                with dve.Fori(1 if first else 0, HALF // 2) as jj:
                    for u in range(2):
                        x_slot(2 * jj + u, u)
                bx_split(b + 1)
                with dve.Fori(HALF // 2, HALF) as jj:
                    for u in range(2):
                        j = 2 * jj + u
                        a_split(b + 1, j, u)
                        join_x(b + 1, 1 - par, j, u)
                        split_w(b * C + j + 1, 1 - u)
                        add_delta(b + 1, j, u)
                        h_split(b + 1, 1 - par, j, u)
                        finish_y(b, par, j, u)

            batch(0, 0, first=True)
            batch(1, 1)
            with dve.Fori(1, NB // 2 - 1) as pair:
                for par in range(2):
                    batch(2 * pair + par, par)
            batch(NB - 2, 0)
            batch(NB - 1, 1, prep=False)

        @block.tensor
        def _(pe):
            def low_rank_in(bp, par, j, u):
                pe.wait_ge(lr_zeroed, bp + 1)
                pe.wait_ge(lo_done, bp * C + j + 1)
                for c in range(2):
                    cols = lr_stk[u][:, c, :, :, :, :].rearrange("p w d s r -> p (w d s r)")
                    for x in (h_hi[par], h_lo[par]):
                        pe.matmul(lr_ps[:, :], cols,
                                  x[:, bass.ds(2 * j + c, 1), :].rearrange("p a n -> p (a n)"),
                                  start=False, stop=False, skip_group_check=True)
                for c in range(2):
                    last = pe.matmul(g_ps[:, :], a0_stk[u][:, c, :, :].rearrange("p a r -> p (a r)"),
                                     lr_stk[u][:, c, 1, 0, :, :].rearrange("p s r -> p (s r)"),
                                     start=False, stop=False, skip_group_check=True)
                last.then_inc(prep_mm_done, 1)

            def low_rank_join(bp):
                pe.wait_ge(bx_done, bp + 1)
                pe.wait_ge(g_lo_done, bp + 1)
                for g in (g_hi, g_lo):
                    last = pe.matmul(lr_ps[:, :], g[:, :, :, :, :].rearrange("p w d s r -> p (w d s r)"),
                                     bx_stk[:, :], start=False, stop=True, skip_group_check=True)
                last.then_inc(xr_done, 1)

            def h_delta(bp, j, u, first=False):
                n = bp * HALF + j - HALF
                pe.wait_ge(bx_done, bp + 1)
                pe.wait_ge(a_lo_done, n + 1)
                if not first:
                    pe.wait_ge(h_added, n)
                for c in range(2):
                    last = pe.matmul(hd_ps[:, c, :], a_stk[u][:, c * P:(c + 1) * P], bx_stk[:, :],
                                     start=True, stop=True)
                last.then_inc(hd_done, 1)

            def main(b, par, j, u, chunks):
                for c in chunks:
                    if c == 0:
                        pe.wait_ge(w_lo_done, b * C + j + 1)
                    for w, h in ((w_hi, h_hi), (w_hi, h_lo), (w_lo, h_hi)):
                        pe.matmul(y_ps[u][:, :], w[u][:, c, :], h[par][:, c, :],
                                  start=(c == 0 and w is w_hi and h is h_hi), stop=False)

            def low_rank_out(b, u):
                pe.wait_ge(xr_stacked, b + 1)
                pe.matmul(y_ps[u][:, :], w_hi[u][:, C, :], xr_stk[:, :], start=False, stop=True
                          ).then_inc(main_done, 1)

            def slot(b, par, j, u):
                pe.wait_ge(lo_done, (b + 1) * C - 1)
                main(b, par, j, u, range(C - 2))
                pe.wait_ge(lo_done, (b + 1) * C)
                main(b, par, j, u, range(C - 2, C))
                low_rank_out(b, u)

            def batch(b, par, prep=True, first=False):
                if not prep:
                    with pe.Fori(0, HALF) as jj:
                        for u in range(2):
                            slot(b, par, 2 * jj + u, u)
                    return
                if first:
                    low_rank_in(b + 1, 1 - par, 0, 0)
                    for j, steps in ((2, (1, 2)), (3, (3,))):
                        slot(b, par, j, j % 2)
                        for j in steps:
                            low_rank_in(b + 1, 1 - par, j, j % 2)
                with pe.Fori(2 if first else 0, HALF // 2) as jj:
                    for u in range(2):
                        slot(b, par, 2 * jj + u, u)
                        low_rank_in(b + 1, 1 - par, 2 * jj + u, u)
                with pe.Fori(HALF // 2, HALF) as jj:
                    for u in range(2):
                        j = 2 * jj + u
                        main(b, par, j, u, range(LEAD))
                        h_delta(b + 1, j, u)
                        main(b, par, j, u, range(LEAD, C))
                        low_rank_out(b, u)
                low_rank_join(b + 1)

            pe.sem_inc(main_done, 1)
            with pe.Fori(0, HALF // 2) as jj:
                for u in range(2):
                    low_rank_in(0, 0, 2 * jj + u, u)
            h_delta(0, HALF, 0, first=True)
            low_rank_join(0)
            for k in range(HALF):
                if k + 1 < HALF:
                    h_delta(0, HALF + k + 1, (k + 1) % 2)
                pe.wait_ge(lo_done, HALF + k + 1)
                for u in range(2):
                    main(0, 0, u, u, (2 * k, 2 * k + 1))
                    if k + 1 == HALF:
                        low_rank_out(0, u)
            batch(0, 0, first=True)
            batch(1, 1)
            with pe.Fori(1, NB // 2 - 1) as pair:
                for par in range(2):
                    batch(2 * pair + par, par)
            batch(NB - 2, 0)
            batch(NB - 1, 1, prep=False)


_INS = ["xT", "ids0", "ids1", "A0", "A0n", "B0", "W", "A1", "B1"]


def kernel(x, itok_B_3_7, itok_B_0_15, L0_cond_A, L0_cond_B, L1_cond_W, L1_cond_lora_A, L1_cond_lora_B):
    import numpy as np
    import concourse.bacc as bacc
    from concourse.bass_utils import run_bass_kernel_spmd

    nb, n, d = x.shape
    c = d // P
    a0, b0, w, a1, b1 = (np.asarray(v) for v in (L0_cond_A, L0_cond_B, L1_cond_W, L1_cond_lora_A,
                                                 L1_cond_lora_B))
    r = a0.shape[2]
    laid = {
        "xT": np.asarray(x).transpose(0, 2, 1).reshape(nb, c // 2, 2, P, n).transpose(0, 1, 3, 2, 4)
                           .reshape(nb * c // 2, P, 2, n),
        "ids0": np.asarray(itok_B_3_7).reshape(1, nb),
        "ids1": np.asarray(itok_B_0_15).reshape(1, nb),
        "A0": a0.transpose(0, 2, 1),
        "A0n": a0.reshape(-1, c, P, r).transpose(0, 2, 1, 3),
        "B0": b0.reshape(-1, r, c, P).transpose(0, 3, 2, 1),
        "W": w.reshape(c, P, c, P).transpose(2, 1, 0, 3),
        "A1": a1.reshape(-1, c, P, r).transpose(0, 2, 1, 3),
        "B1": b1,
    }
    nc = bacc.Bacc("TRN2", target_bir_lowering=False, num_devices=1)
    arrays, args = {}, []
    for name in _INS:
        a = np.ascontiguousarray(laid[name])
        arrays[f"in_{name}"] = a
        args.append(nc.dram_tensor(f"in_{name}", a.shape, mybir.dt.from_np(a.dtype), kind="ExternalInput").ap())
    out = nc.dram_tensor("out_y", (nb * c, P, n), F32, kind="ExternalOutput").ap()
    lora_residual_program(nc, *args, out)
    got = run_bass_kernel_spmd(nc, [arrays], core_ids=[0]).results[0]["out_y"]
    return np.ascontiguousarray(got.reshape(nb, d, n).transpose(0, 2, 1))
```

```python
from contextlib import ExitStack

import concourse.bass as bass
from concourse import mybir

F32 = mybir.dt.float32
F32R = mybir.dt.float32r
I32 = mybir.dt.int32
ALU = mybir.AluOpType

P = 128


def lora_residual_program(nc, xT, ids0, ids1, A0, A0n, B0, W, A1, B1, yT):
    NB = ids0.shape[1]
    NA0, R, D = A0.shape
    NA1 = B1.shape[0]
    C = D // P
    N = xT.shape[3]
    HALF = C // 2
    REP = P // R
    BANDS = 4
    BAND = P // BANDS
    X0 = 6 + 2 * C // (N // P)
    LEAD = 9

    with ExitStack() as ctx:
        def sb(name, shape, dt=F32):
            return ctx.enter_context(nc.sbuf_tensor(name, shape, dt))

        def pb(name, shape):
            return ctx.enter_context(nc.psum_tensor(name, shape, F32))

        def sem(name):
            return ctx.enter_context(nc.semaphore(name))

        h_hi = [sb(f"h_hi{i}", [P, C, N], F32R) for i in range(2)]
        h_lo = [sb(f"h_lo{i}", [P, C, N], F32R) for i in range(2)]
        w_raw = [sb(f"w_raw{i}", [P, C + 1, P]) for i in range(2)]
        w_hi = [sb(f"w_hi{i}", [P, C + 1, P], F32R) for i in range(2)]
        w_lo = [sb(f"w_lo{i}", [P, C, P], F32R) for i in range(2)]
        xh = [sb(f"xh{i}", [P, 2, N]) for i in range(2)]
        b_raw = sb("b_raw", [P, C, R])
        a1_raw = sb("a1_raw", [P, C, R])
        a0_raw = sb("a0_raw", [P, C, R])
        lr_stk = [sb(f"lr_stk{i}", [P, 2, 2, 2, 2, R], F32R) for i in range(2)]
        a0_stk = [sb(f"a0_stk{i}", [P, 2, REP, R], F32R) for i in range(2)]
        g_hi = sb("g_hi", [P, 2, 2, 2, R], F32R)
        g_lo = sb("g_lo", [P, 2, 2, 2, R], F32R)
        a_raw = [sb(f"a_raw{i}", [P, 2 * P]) for i in range(2)]
        a_stk = [sb(f"a_stk{i}", [P, 2 * P], F32R) for i in range(2)]
        bx_stk = sb("bx_stk", [P, N], F32R)
        xr_stk = sb("xr_stk", [P, N], F32R)
        y_out = sb("y_out", [P, 2, N])
        ids = sb("ids", [1, 2, NB], I32)

        y_ps = [pb(f"y_ps{i}", [P, N]) for i in range(2)]
        hd_ps = [pb(f"hd_ps{i}", [P, 2, N]) for i in range(2)]
        lr_ps = pb("lr_ps", [P, N])
        g_ps = pb("g_ps", [P, 2 * R])

        ids_loaded = sem("ids_loaded")
        w_loaded = [sem(f"w_loaded{i}") for i in range(2)]
        x0_loaded = [sem(f"x0_loaded{i}") for i in range(X0)]
        x_loaded = [sem(f"x_loaded{i}") for i in range(2)]
        a_loaded = [sem(f"a_loaded{i}") for i in range(2)]
        b_loaded = sem("b_loaded")
        a1_loaded = sem("a1_loaded")
        a0_loaded = sem("a0_loaded")
        y_stored = [sem(f"y_stored{i}") for i in range(2)]
        w_hi_done = sem("w_hi_done")
        w_lo_done = sem("w_lo_done")
        main_done = sem("main_done")
        y_hi_added = sem("y_hi_added")
        y_done = sem("y_done")
        lr_hi_done = sem("lr_hi_done")
        x0_hi_done = sem("x0_hi_done")
        x0_lo_done = sem("x0_lo_done")
        x_hi_done = sem("x_hi_done")
        prep_mm_done = sem("prep_mm_done")
        a_hi_done = sem("a_hi_done")
        a_lo_done = sem("a_lo_done")
        x_joined = sem("x_joined")
        hd_done = sem("hd_done")
        h_added = sem("h_added")
        h_hi_done = sem("h_hi_done")
        lo_done = sem("lo_done")
        g_hi_done = sem("g_hi_done")
        g_lo_done = sem("g_lo_done")
        bx_hi_done = sem("bx_hi_done")
        bx_lo_done = sem("bx_lo_done")
        bx_done = sem("bx_done")
        xr_done = sem("xr_done")
        xr_hi_done = sem("xr_hi_done")
        xr_lo_done = sem("xr_lo_done")
        xr_stacked = sem("xr_stacked")
        lr_zeroed = sem("lr_zeroed")

        x0_raw = [xh[i // 2][:, i % 2, :] for i in range(4)]
        x0_raw += [w_raw[u][:, i:i + N // P, :].rearrange("p c n -> p (c n)")
                   for u in range(2) for i in range(0, C, N // P)]
        x0_raw += [y_out[:, i, :] for i in range(2)]
        assert len(x0_raw) == X0
        pairs = [xh[i][:, :, :] for i in range(2)]
        pairs += [w_raw[u][:, i:i + 2 * N // P, :].rearrange("p (a c) n -> p a (c n)", a=2)
                  for u in range(2) for i in range(0, C, 2 * N // P)]
        pairs += [y_out[:, :, :]]
        h0_pairs = (0, 1, 6, 4, 5, 0, 1, 6)
        assert len(h0_pairs) == HALF and 2 * len(pairs) == X0
        h0 = [pairs[i] for i in h0_pairs]

        def h0_loaded(k):
            i = h0_pairs[k]
            chunks = len(range(2 * i, C, X0))
            return x0_loaded[2 * i], 16 * (chunks + h0_pairs[:k + 1].count(i))

        def x0_split_count(c):
            return (lambda done: (done, c // 2 + 1))((x0_lo_done, lo_done)[c % 2])

        block = ctx.enter_context(nc.Block())

        def two(chunk):
            return bass.ds(chunk, 2)

        @block.sync
        def _(sp):
            def load_x0(c):
                if c >= X0:
                    sp.wait_ge(*x0_split_count(c - X0))
                sp.dma_start(x0_raw[c % X0], xT[c // 2, :, c % 2, :]).then_inc(x0_loaded[c % X0], 16)

            sp.dma_start(ids[:, 0, :], ids0).then_inc(ids_loaded, 16)
            sp.dma_start(ids[:, 1, :], ids1).then_inc(ids_loaded, 16)
            for c in range(4):
                load_x0(c)
            sp.wait_ge(ids_loaded, 32)

            def id0(b):
                return sp.value_load(ids[0:1, 0, bass.ds(b, 1)], min_val=0, max_val=NA0 - 1)

            def id1(b):
                return sp.value_load(ids[0:1, 1, bass.ds(b, 1)], min_val=0, max_val=NA1 - 1)

            def load_h0(k):
                if k < 3:
                    sp.wait_ge(lo_done, HALF)
                elif h0_pairs[k] in (4, 5):
                    sp.wait_ge(w_lo_done, 2)
                else:
                    sp.wait_ge(lo_done, HALF + h0_pairs.index(h0_pairs[k]) + 1)
                sp.dma_start(h0[k], xT[k, :, :, :]).then_inc(h0_loaded(k)[0], 16)

            def rows_rep(dst, src):
                return dst, src.unsqueeze(0).broadcast_to([REP, R, src.shape[-1]])

            def load_w(b, j, u, a1, first=False):
                if not first:
                    sp.wait_ge(w_lo_done, b * C + j - 1)
                sp.dma_start(w_raw[u][:, 0:C, :], W[bass.ds(j, 1), :, :, :].rearrange("a p c n -> (a p) c n")
                             ).then_inc(w_loaded[u], 16)
                dst, src = rows_rep(w_raw[u][:, C, :], B1[bass.ds(a1, 1), :, bass.ds(j * P, P)]
                                    .rearrange("a r n -> (a r) n"))
                sp.dma_start(dst, src).then_inc(w_loaded[u], 16)

            def load_x(bp, j, u):
                sp.wait_ge(lo_done, bp * C + j - 1)
                sp.dma_start(xh[u][:, :, :], xT[bass.ds(bp * HALF + j, 1), :, :, :]
                             .rearrange("a p c n -> (a p) c n")).then_inc(x_loaded[u], 16)

            def load_a(bp, k, u, a0, first=False):
                if not first:
                    sp.wait_ge(a_lo_done, bp * HALF + k - 1)
                dst, src = rows_rep(a_raw[u][:, :], A0[bass.ds(a0, 1), :, bass.ds(k * 2 * P, 2 * P)]
                                    .rearrange("a r n -> (a r) n"))
                sp.dma_start(dst, src).then_inc(a_loaded[u], 16)

            def load_low_rank(bp, a0, a1, first=False):
                if not first:
                    sp.wait_ge(prep_mm_done, bp * HALF)
                for dst, src, a, loaded in ((b_raw, B0, a0, b_loaded), (a1_raw, A1, a1, a1_loaded),
                                            (a0_raw, A0n, a0, a0_loaded)):
                    sp.dma_start(dst[:, :, :], src[bass.ds(a, 1), :, :, :].rearrange("a p c r -> (a p) c r")
                                 ).then_inc(loaded, 16)

            def store_y(s, u):
                sp.wait_ge(y_done, s + 1)
                sp.dma_start(yT[bass.ds(s, 1), :, :].rearrange("a p n -> (a p) n"), y_out[:, u, :]
                             ).then_inc(y_stored[u], 16)

            for u in range(2):
                sp.sem_inc(y_stored[u], 1)
            a0, a1 = id0(0), id1(0)
            load_low_rank(0, a0, a1, first=True)
            for c in range(4, C):
                load_x0(c)
            for u in range(2):
                load_a(0, u, u, a0, first=True)
            for u in range(2):
                sp.wait_ge(*x0_split_count(4 + (u + 1) * C // (N // P) - 1))
                load_w(0, u, u, a1, first=True)
            for k in range(3):
                load_h0(k)
            for k in range(2, 5):
                load_a(0, k, k % 2, a0)
            for k in range(3, 5):
                load_h0(k)
            load_a(0, 5, 1, a0)
            for k in range(5, HALF):
                load_h0(k)
                if k + 1 < HALF:
                    load_a(0, k + 1, (k + 1) % 2, a0)
            load_w(0, 2, 0, a1)
            sp.wait_ge(lo_done, HALF + h0_pairs.index(5) + 1)
            load_w(0, 3, 1, a1)

            def batch(b, prep=True, first=False):
                a1_now = id1(b)
                if prep:
                    a0, a1 = id0(b + 1), id1(b + 1)
                    load_low_rank(b + 1, a0, a1)

                def slot(jj, u, kind):
                    j = 2 * jj + u
                    if not (first and isinstance(j, int) and j < 4):
                        load_w(b, j, u, a1_now)
                    if kind == "x":
                        load_x(b + 1, j, u)
                    elif kind == "h":
                        load_a(b + 1, j - HALF, u, a0)
                    if not (first and isinstance(j, int) and j < 3):
                        store_y(b * C + j - 3, 1 - u)

                ahead = 2 if first else 0
                for jj in range(ahead):
                    for u in range(2):
                        slot(jj, u, "x")
                if prep:
                    with sp.Fori(ahead, HALF // 2) as jj:
                        for u in range(2):
                            slot(jj, u, "x")
                    with sp.Fori(HALF // 2, HALF) as jj:
                        for u in range(2):
                            slot(jj, u, "h")
                else:
                    with sp.Fori(0, HALF) as jj:
                        for u in range(2):
                            slot(jj, u, None)

            batch(0, first=True)
            with sp.Fori(1, NB - 1) as b:
                batch(b)
            batch(NB - 1, prep=False)
            for s in range(NB * C - 3, NB * C):
                store_y(s, s % 2)
            for u in range(2):
                sp.wait_ge(y_stored[u], 16 * (NB * C // 2) + 1)

        @block.scalar
        def _(act):
            def split_w(s, u, first=False):
                act.wait_ge(w_loaded[u], (s - u) * 16 + 32)
                if not first:
                    act.wait_ge(main_done, s)
                act.copy(w_hi[u][:, :, :], w_raw[u][:, :, :]).then_inc(w_hi_done, 1)

            def low_rank_split(bp, j, u, first=False):
                if not first:
                    act.wait_ge(prep_mm_done, bp * HALF + j - 1)
                for which, (raw, loaded) in enumerate(((b_raw, b_loaded), (a1_raw, a1_loaded))):
                    act.wait_ge(loaded, bp * 16 + 16)
                    act.copy(lr_stk[u][:, :, which, :, 0, :],
                             raw[:, two(2 * j), :].unsqueeze(2).broadcast_to([P, 2, 2, R]))
                act.wait_ge(a0_loaded, bp * 16 + 16)
                act.copy(a0_stk[u][:, :, :, :],
                         a0_raw[:, two(2 * j), :].unsqueeze(2).broadcast_to([P, 2, REP, R])
                         ).then_inc(lr_hi_done, 1)

            def x0_step(j):
                for c in (2 * j, 2 * j + 1):
                    act.wait_ge(x0_loaded[c % X0], 16 * (c // X0 + 1))
                    act.copy(h_hi[0][:, c, :], x0_raw[c % X0]).then_inc(x0_hi_done, 1)
                low_rank_split(0, j, j % 2, first=(j < 2))

            def x_step(bp, par, j, u):
                low_rank_split(bp, j, u)
                act.wait_ge(x_loaded[u], ((bp - 1) * HALF + j - u) * 8 + 16)
                act.copy(h_hi[par][:, two(2 * j), :], xh[u][:, :, :]).then_inc(x_hi_done, 1)

            def bx_split(bp):
                act.wait_ge(prep_mm_done, (bp + 1) * HALF)
                act.copy(bx_stk[0:P // 2, :], lr_ps[0:P // 2, :]).then_inc(bx_hi_done, 1)
                act.copy(g_hi[:, 1, :, :, :].rearrange("p d s r -> p d (s r)"),
                         g_ps[:, :].unsqueeze(1).broadcast_to([P, 2, 2 * R])).then_inc(g_hi_done, 1)
                act.wait_ge(bx_lo_done, bp + 1)
                act.copy(bx_stk[P // 2:P, :], bx_stk[0:P // 2, :].bitcast(F32)).then_inc(bx_done, 1)

            def a_split(bp, j, u, first=False):
                n = bp * HALF + j - HALF
                act.wait_ge(a_loaded[u], (n - u) * 8 + 16)
                if not first:
                    act.wait_ge(hd_done, n - 1)
                act.copy(a_stk[u][:, :], a_raw[u][:, :]).then_inc(a_hi_done, 1)

            def h_split(bp, par, j, u):
                k = j - HALF
                act.wait_ge(h_added, bp * HALF + k + 1)
                act.copy(h_hi[par][:, two(2 * k), :], xh[u][:, :, :]).then_inc(h_hi_done, 1)

            def xr_split(b):
                act.wait_ge(xr_done, b + 1)
                act.copy(xr_stk[P // 2:P, :], lr_ps[P // 2:P, :]).then_inc(xr_hi_done, 1)
                act.wait_ge(xr_lo_done, b + 1)
                act.copy(xr_stk[0:P // 2, :], xr_stk[P // 2:P, :].bitcast(F32)).then_inc(xr_stacked, 1)

            for j in range(HALF):
                x0_step(j)
            a_split(0, HALF, 0, first=True)
            a_split(0, HALF + 1, 1, first=True)
            split_w(0, 0, first=True)
            bx_split(0)
            split_w(1, 1, first=True)
            a_split(0, HALF + 2, 0)
            for k in range(HALF):
                act.wait_ge(h_added, k + 1)
                act.copy(h_hi[0][:, 2 * k:2 * k + 2, :], h0[k]).then_inc(h_hi_done, 1)
                if k + 3 < HALF:
                    a_split(0, HALF + k + 3, (k + 3) % 2)
                if k == 1:
                    xr_split(0)

            def batch(b, par, prep=True, first=False):
                def x_slot(j, u, w_split=True):
                    if w_split:
                        split_w(b * C + j + 1, 1 - u)
                    x_step(b + 1, 1 - par, j, u)

                if not first:
                    xr_split(b)
                    if prep:
                        act.wait_ge(xr_lo_done, b + 1)
                if not prep:
                    split_w(b * C + 1, 1)
                    with act.Fori(1, HALF) as jj:
                        for u in range(2):
                            split_w(b * C + 2 * jj + u, u)
                    return
                if first:
                    x_slot(0, 0, w_split=False)
                    x_slot(1, 1)
                with act.Fori(1 if first else 0, HALF // 2) as jj:
                    for u in range(2):
                        x_slot(2 * jj + u, u)
                bx_split(b + 1)
                with act.Fori(HALF // 2, HALF) as jj:
                    for u in range(2):
                        j = 2 * jj + u
                        a_split(b + 1, j, u)
                        split_w(b * C + j + 1, 1 - u)
                        h_split(b + 1, 1 - par, j, u)

            batch(0, 0, first=True)
            batch(1, 1)
            with act.Fori(1, NB // 2 - 1) as pair:
                for par in range(2):
                    batch(2 * pair + par, par)
            batch(NB - 2, 0)
            batch(NB - 1, 1, prep=False)

        @block.vector
        def _(dve):
            def split_w(s, u):
                dve.wait_ge(w_hi_done, s + 1)
                dve.tensor_tensor(w_hi[u][P // 2:P, C, :], w_raw[u][P // 2:P, C, :],
                                  w_hi[u][P // 2:P, C, :].bitcast(F32), ALU.subtract)
                dve.tensor_tensor(w_lo[u][:, :, :], w_raw[u][:, 0:C, :],
                                  w_hi[u][:, 0:C, :].bitcast(F32), ALU.subtract).then_inc(w_lo_done, 1)

            def low_rank_split(bp, j, u):
                dve.wait_ge(lr_hi_done, bp * HALF + j + 1)
                for which, raw in enumerate((b_raw, a1_raw)):
                    dve.tensor_tensor(lr_stk[u][:, :, which, :, 1, :],
                                      raw[:, two(2 * j), :].unsqueeze(2).broadcast_to([P, 2, 2, R]),
                                      lr_stk[u][:, :, which, :, 0, :].bitcast(F32), ALU.subtract)
                dve.tensor_tensor(a0_stk[u][:, :, REP // 2:REP, :],
                                  a0_raw[:, two(2 * j), :].unsqueeze(2).broadcast_to([P, 2, REP // 2, R]),
                                  a0_stk[u][:, :, REP // 2:REP, :].bitcast(F32), ALU.subtract)

            def x0_step(j):
                for c in (2 * j, 2 * j + 1):
                    dve.wait_ge(x0_hi_done, c + 1)
                    dve.tensor_tensor(h_lo[0][:, c, :], x0_raw[c % X0], h_hi[0][:, c, :].bitcast(F32),
                                      ALU.subtract).then_inc(x0_split_count(c)[0], 1)
                    if c == 2 * j:
                        low_rank_split(0, j, j % 2)

            def x_step(bp, par, j, u):
                low_rank_split(bp, j, u)
                dve.wait_ge(x_hi_done, (bp - 1) * HALF + j + 1)
                dve.tensor_tensor(h_lo[par][:, two(2 * j), :], xh[u][:, :, :],
                                  h_hi[par][:, two(2 * j), :].bitcast(F32), ALU.subtract).then_inc(lo_done, 1)

            def bx_split(bp):
                dve.wait_ge(bx_hi_done, bp + 1)
                dve.tensor_tensor(bx_stk[BAND:2 * BAND, :], lr_ps[BAND:2 * BAND, :],
                                  bx_stk[BAND:2 * BAND, :].bitcast(F32), ALU.subtract).then_inc(bx_lo_done, 1)
                dve.wait_ge(g_hi_done, bp + 1)
                dve.tensor_tensor(g_lo[:, 1, :, :, :].rearrange("p d s r -> p d (s r)"),
                                  g_ps[:, :].unsqueeze(1).broadcast_to([P, 2, 2 * R]),
                                  g_hi[:, 1, :, :, :].rearrange("p d s r -> p d (s r)").bitcast(F32),
                                  ALU.subtract).then_inc(g_lo_done, 1)
                dve.wait_ge(g_lo_done, bp + 1)
                dve.memset(g_ps[:, :], 0.0)

            def a_split(bp, j, u):
                dve.wait_ge(a_hi_done, bp * HALF + j - HALF + 1)
                dve.tensor_tensor(a_stk[u][P // 2:P, :], a_raw[u][P // 2:P, :],
                                  a_stk[u][P // 2:P, :].bitcast(F32), ALU.subtract).then_inc(a_lo_done, 1)

            def join_x(bp, par, j, u):
                k = j - HALF
                dve.wait_ge(lo_done, bp * C + HALF)
                dve.wait_ge(lo_done, bp * C + j - 1)
                dve.tensor_tensor(xh[u][:, :, :], h_hi[par][:, two(2 * k), :].bitcast(F32),
                                  h_lo[par][:, two(2 * k), :].bitcast(F32), ALU.add).then_inc(x_joined, 1)

            def a_split(bp, j, u):
                dve.wait_ge(a_hi_done, bp * HALF + j - HALF + 1)
                dve.tensor_tensor(a_stk[u][P // 2:P, :], a_raw[u][P // 2:P, :],
                                  a_stk[u][P // 2:P, :].bitcast(F32), ALU.subtract).then_inc(a_lo_done, 1)

            def add_delta(bp, j, u):
                n = bp * HALF + j - HALF
                dve.wait_ge(x_joined, n + 1 - HALF)
                dve.wait_ge(hd_done, n + 1)
                dve.tensor_tensor(xh[u][:, :, :], hd_ps[u][:, :, :], xh[u][:, :, :], ALU.add).then_inc(h_added, 1)

            def h_split(bp, par, j, u):
                k = j - HALF
                n = bp * HALF + k
                dve.wait_ge(h_hi_done, n + 1)
                dve.tensor_tensor(h_lo[par][:, two(2 * k), :], xh[u][:, :, :],
                                  h_hi[par][:, two(2 * k), :].bitcast(F32), ALU.subtract).then_inc(lo_done, 1)

            def xr_split(b):
                dve.wait_ge(xr_hi_done, b + 1)
                dve.tensor_tensor(xr_stk[3 * BAND:P, :], lr_ps[3 * BAND:P, :],
                                  xr_stk[3 * BAND:P, :].bitcast(F32), ALU.subtract).then_inc(xr_lo_done, 1)
                dve.wait_ge(xr_lo_done, b + 1)
                dve.memset(lr_ps[:, :], 0.0).then_inc(lr_zeroed, 1)

            def finish_y(b, par, j, u):
                s = b * C + j
                dve.wait_ge(main_done, s + 2)
                dve.wait_ge(y_stored[u], (s - u) * 8 + 1)
                one = bass.ds(j, 1)
                dve.tensor_tensor(y_out[:, u, :], y_ps[u][:, :],
                                  h_hi[par][:, one, :].rearrange("p a n -> p (a n)").bitcast(F32),
                                  ALU.add).then_inc(y_hi_added, 1)
                dve.wait_ge(y_hi_added, s + 1)
                dve.tensor_tensor(y_out[:, u, :], y_out[:, u, :],
                                  h_lo[par][:, one, :].rearrange("p a n -> p (a n)").bitcast(F32),
                                  ALU.add).then_inc(y_done, 1)

            dve.memset(g_ps[:, :], 0.0)
            dve.memset(lr_ps[:, :], 0.0).then_inc(lr_zeroed, 1)
            dve.memset(g_hi[:, 0, :, :, :].bitcast(F32), 0.0)
            dve.memset(g_lo[:, 0, :, :, :].bitcast(F32), 0.0)

            for j in range(HALF):
                x0_step(j)
            a_split(0, HALF, 0)
            a_split(0, HALF + 1, 1)
            bx_split(0)
            split_w(0, 0)

            def add_delta0(k):
                dve.wait_ge(*h0_loaded(k))
                dve.wait_ge(hd_done, k + 1)
                dve.tensor_tensor(h0[k], hd_ps[k % 2][:, :, :], h0[k], ALU.add).then_inc(h_added, 1)

            add_delta0(0)
            a_split(0, HALF + 2, 0)
            for k in range(HALF):
                if k + 1 < HALF:
                    add_delta0(k + 1)
                dve.wait_ge(h_hi_done, k + 1)
                dve.tensor_tensor(h_lo[0][:, 2 * k:2 * k + 2, :], h0[k],
                                  h_hi[0][:, 2 * k:2 * k + 2, :].bitcast(F32), ALU.subtract).then_inc(lo_done, 1)
                if k == 0:
                    split_w(1, 1)
                if k + 3 < HALF:
                    a_split(0, HALF + k + 3, (k + 3) % 2)
                if k == 1:
                    xr_split(0)

            def batch(b, par, prep=True, first=False):
                def x_slot(j, u, w_split=True):
                    if w_split:
                        split_w(b * C + j + 1, 1 - u)
                    x_step(b + 1, 1 - par, j, u)
                    finish_y(b, par, j, u)

                if not first:
                    xr_split(b)
                if not prep:
                    with dve.Fori(0, HALF - 1) as jj:
                        for u in range(2):
                            j = 2 * jj + u
                            split_w(b * C + j + 1, 1 - u)
                            finish_y(b, par, j, u)
                    split_w(b * C + C - 1, 1)
                    for j in range(C - 2, C):
                        finish_y(b, par, j, j % 2)
                    return
                if first:
                    x_slot(0, 0, w_split=False)
                    x_slot(1, 1)
                with dve.Fori(1 if first else 0, HALF // 2) as jj:
                    for u in range(2):
                        x_slot(2 * jj + u, u)
                bx_split(b + 1)
                with dve.Fori(HALF // 2, HALF) as jj:
                    for u in range(2):
                        j = 2 * jj + u
                        a_split(b + 1, j, u)
                        split_w(b * C + j + 1, 1 - u)
                        join_x(b + 1, 1 - par, j, u)
                        add_delta(b + 1, j, u)
                        h_split(b + 1, 1 - par, j, u)
                        finish_y(b, par, j, u)

            batch(0, 0, first=True)
            batch(1, 1)
            with dve.Fori(1, NB // 2 - 1) as pair:
                for par in range(2):
                    batch(2 * pair + par, par)
            batch(NB - 2, 0)
            batch(NB - 1, 1, prep=False)

        @block.tensor
        def _(pe):
            def low_rank_in(bp, par, j, u):
                pe.wait_ge(lr_zeroed, bp + 1)
                pe.wait_ge(lo_done, bp * C + j + 1)
                for c in range(2):
                    cols = lr_stk[u][:, c, :, :, :, :].rearrange("p w d s r -> p (w d s r)")
                    for x in (h_hi[par], h_lo[par]):
                        pe.matmul(lr_ps[:, :], cols,
                                  x[:, bass.ds(2 * j + c, 1), :].rearrange("p a n -> p (a n)"),
                                  start=False, stop=False, skip_group_check=True)
                for c in range(2):
                    last = pe.matmul(g_ps[:, :], a0_stk[u][:, c, :, :].rearrange("p a r -> p (a r)"),
                                     lr_stk[u][:, c, 1, 0, :, :].rearrange("p s r -> p (s r)"),
                                     start=False, stop=False, skip_group_check=True)
                last.then_inc(prep_mm_done, 1)

            def low_rank_join(bp):
                pe.wait_ge(bx_done, bp + 1)
                pe.wait_ge(g_lo_done, bp + 1)
                for g in (g_hi, g_lo):
                    last = pe.matmul(lr_ps[:, :], g[:, :, :, :, :].rearrange("p w d s r -> p (w d s r)"),
                                     bx_stk[:, :], start=False, stop=True, skip_group_check=True)
                last.then_inc(xr_done, 1)

            def h_delta(bp, j, u, first=False):
                n = bp * HALF + j - HALF
                pe.wait_ge(bx_done, bp + 1)
                pe.wait_ge(a_lo_done, n + 1)
                if not first:
                    pe.wait_ge(h_added, n - 1)
                for c in range(2):
                    last = pe.matmul(hd_ps[u][:, c, :], a_stk[u][:, c * P:(c + 1) * P], bx_stk[:, :],
                                     start=True, stop=True)
                last.then_inc(hd_done, 1)

            def main(b, par, j, u, chunks):
                for c in chunks:
                    if c == 0:
                        pe.wait_ge(w_lo_done, b * C + j + 1)
                    for w, h in ((w_hi, h_hi), (w_hi, h_lo), (w_lo, h_hi)):
                        pe.matmul(y_ps[u][:, :], w[u][:, c, :], h[par][:, c, :],
                                  start=(c == 0 and w is w_hi and h is h_hi), stop=False)

            def low_rank_out(b, u):
                pe.wait_ge(xr_stacked, b + 1)
                pe.matmul(y_ps[u][:, :], w_hi[u][:, C, :], xr_stk[:, :], start=False, stop=True
                          ).then_inc(main_done, 1)

            def slot(b, par, j, u):
                pe.wait_ge(lo_done, (b + 1) * C - 1)
                main(b, par, j, u, range(C - 2))
                pe.wait_ge(lo_done, (b + 1) * C)
                main(b, par, j, u, range(C - 2, C))
                low_rank_out(b, u)

            def batch(b, par, prep=True, first=False):
                if not prep:
                    with pe.Fori(0, HALF) as jj:
                        for u in range(2):
                            slot(b, par, 2 * jj + u, u)
                    return
                if first:
                    low_rank_in(b + 1, 1 - par, 0, 0)
                    for j, steps in ((2, (1, 2)), (3, (3,))):
                        slot(b, par, j, j % 2)
                        for j in steps:
                            low_rank_in(b + 1, 1 - par, j, j % 2)
                with pe.Fori(2 if first else 0, HALF // 2) as jj:
                    for u in range(2):
                        slot(b, par, 2 * jj + u, u)
                        low_rank_in(b + 1, 1 - par, 2 * jj + u, u)
                with pe.Fori(HALF // 2, HALF) as jj:
                    for u in range(2):
                        j = 2 * jj + u
                        main(b, par, j, u, range(LEAD))
                        h_delta(b + 1, j, u)
                        main(b, par, j, u, range(LEAD, C))
                        low_rank_out(b, u)
                low_rank_join(b + 1)

            pe.sem_inc(main_done, 1)
            with pe.Fori(0, HALF // 2) as jj:
                for u in range(2):
                    low_rank_in(0, 0, 2 * jj + u, u)
            h_delta(0, HALF, 0, first=True)
            h_delta(0, HALF + 1, 1, first=True)
            low_rank_join(0)
            for k in range(HALF):
                if k + 2 < HALF:
                    h_delta(0, HALF + k + 2, k % 2)
                pe.wait_ge(lo_done, HALF + k + 1)
                for u in range(2):
                    main(0, 0, u, u, (2 * k, 2 * k + 1))
                    if k + 1 == HALF:
                        low_rank_out(0, u)
            batch(0, 0, first=True)
            batch(1, 1)
            with pe.Fori(1, NB // 2 - 1) as pair:
                for par in range(2):
                    batch(2 * pair + par, par)
            batch(NB - 2, 0)
            batch(NB - 1, 1, prep=False)


_INS = ["xT", "ids0", "ids1", "A0", "A0n", "B0", "W", "A1", "B1"]


def kernel(x, itok_B_3_7, itok_B_0_15, L0_cond_A, L0_cond_B, L1_cond_W, L1_cond_lora_A, L1_cond_lora_B):
    import numpy as np
    import concourse.bacc as bacc
    from concourse.bass_utils import run_bass_kernel_spmd

    nb, n, d = x.shape
    c = d // P
    a0, b0, w, a1, b1 = (np.asarray(v) for v in (L0_cond_A, L0_cond_B, L1_cond_W, L1_cond_lora_A,
                                                 L1_cond_lora_B))
    r = a0.shape[2]
    laid = {
        "xT": np.asarray(x).transpose(0, 2, 1).reshape(nb, c // 2, 2, P, n).transpose(0, 1, 3, 2, 4)
                           .reshape(nb * c // 2, P, 2, n),
        "ids0": np.asarray(itok_B_3_7).reshape(1, nb),
        "ids1": np.asarray(itok_B_0_15).reshape(1, nb),
        "A0": a0.transpose(0, 2, 1),
        "A0n": a0.reshape(-1, c, P, r).transpose(0, 2, 1, 3),
        "B0": b0.reshape(-1, r, c, P).transpose(0, 3, 2, 1),
        "W": w.reshape(c, P, c, P).transpose(2, 1, 0, 3),
        "A1": a1.reshape(-1, c, P, r).transpose(0, 2, 1, 3),
        "B1": b1,
    }
    nc = bacc.Bacc("TRN2", target_bir_lowering=False, num_devices=1)
    arrays, args = {}, []
    for name in _INS:
        a = np.ascontiguousarray(laid[name])
        arrays[f"in_{name}"] = a
        args.append(nc.dram_tensor(f"in_{name}", a.shape, mybir.dt.from_np(a.dtype), kind="ExternalInput").ap())
    out = nc.dram_tensor("out_y", (nb * c, P, n), F32, kind="ExternalOutput").ap()
    lora_residual_program(nc, *args, out)
    got = run_bass_kernel_spmd(nc, [arrays], core_ids=[0]).results[0]["out_y"]
    return np.ascontiguousarray(got.reshape(nb, d, n).transpose(0, 2, 1))
```
